# Optimizing a Trainium2 kernel written in Bass

```python
import numpy as np
import jax
import jax.numpy as jnp

def _softmax(x, axis=-1):
    return jax.nn.softmax(x, axis=axis)

def _gelu(x):
    return jax.nn.gelu(x, approximate=True)

def _silu(x):
    return jax.nn.silu(x)

def _sigmoid(x):
    return jax.nn.sigmoid(x)

def _layernorm(x, axis=-1, eps=1e-05):
    m = jnp.mean(x, axis=axis, keepdims=True)
    v = jnp.var(x, axis=axis, keepdims=True)
    return (x - m) / jnp.sqrt(v + eps)

def _scatter_add(tgt, idx, src, axis=0):
    return tgt.at[idx].add(src)

def _segment_sum(src, seg, n):
    return jax.ops.segment_sum(src, seg, n)
kernel_name = 'mk_seq_postln_d1_jaxref_r8_1e1d17'

def setup_inputs(seed: int=0):
    np.random.seed(seed)
    _w = jnp.asarray

    def _L0_attn_setup():
        import jax, jax.numpy as jnp
        import numpy as np
        B, S, D = (2, 256, 256)
        H, HD = (32, 128)
        P = H * HD
        K = 4
        F_ = 1024
        EPS = 1e-06

        def _rmsnorm(x, w, eps=EPS):
            xf = x.astype(jnp.float32)
            y = xf * jax.lax.rsqrt(jnp.mean(xf * xf, axis=-1, keepdims=True) + eps)
            return (y * w).astype(x.dtype)

        def _short_conv(x, w):
            k = w.shape[1]
            xp = jnp.pad(x, ((0, 0), (k - 1, 0), (0, 0)))
            y = sum((xp[:, j:j + x.shape[1], :] * w[:, j] for j in range(k)))
            return jax.nn.silu(y)

        def _l2norm(x, eps=1e-06):
            return x * jax.lax.rsqrt(jnp.sum(x * x, axis=-1, keepdims=True) + eps)

        def _kda(q, k, v, g, beta):
            scale = q.shape[-1] ** (-0.5)
            q = _l2norm(q) * scale
            k = _l2norm(k)
            tm = lambda a: jnp.swapaxes(a, 0, 1)
            qs, ks_, vs, gs, bs = (tm(q), tm(k), tm(v), tm(g), tm(beta))
            bsz, h, hd = (q.shape[0], q.shape[2], q.shape[3])
            S0 = jnp.zeros((bsz, h, hd, hd), jnp.float32)

            def step(St, inp):
                qt, kt, vt, gt, bt = inp
                St = St * jnp.exp(gt)[..., None]
                err = jnp.einsum('bhk,bhkv->bhv', kt, St)
                St = St + bt[..., None, None] * kt[..., None] * (vt - err)[..., None, :]
                ot = jnp.einsum('bhk,bhkv->bhv', qt, St)
                return (St, ot)
            _, o = jax.lax.scan(step, S0, (qs, ks_, vs, gs, bs))
            return jnp.swapaxes(o, 0, 1)
        key = jax.random.key(seed)
        ks = jax.random.split(key, 20)
        std = 0.02
        inp = {'x': jax.random.normal(ks[0], (B, S, D), jnp.float32), 'norm1_w': jnp.ones((D,), jnp.float32), 'wq': jax.random.normal(ks[1], (D, P), jnp.float32) * std, 'wk': jax.random.normal(ks[2], (D, P), jnp.float32) * std, 'wv': jax.random.normal(ks[3], (D, P), jnp.float32) * std, 'conv_q': jax.random.normal(ks[4], (P, K), jnp.float32) * 0.5, 'conv_k': jax.random.normal(ks[5], (P, K), jnp.float32) * 0.5, 'conv_v': jax.random.normal(ks[6], (P, K), jnp.float32) * 0.5, 'f_a': jax.random.normal(ks[7], (D, HD), jnp.float32) * std, 'f_b': jax.random.normal(ks[8], (HD, P), jnp.float32) * std, 'A_log': jnp.log(jax.random.uniform(ks[9], (H,), jnp.float32, 1.0, 16.0)), 'dt_bias': jnp.zeros((P,), jnp.float32), 'b_w': jax.random.normal(ks[10], (D, H), jnp.float32) * std, 'g_a': jax.random.normal(ks[11], (D, HD), jnp.float32) * std, 'g_b': jax.random.normal(ks[12], (HD, P), jnp.float32) * std, 'onorm_w': jnp.ones((HD,), jnp.float32), 'wo': jax.random.normal(ks[13], (P, D), jnp.float32) * std, 'norm2_w': jnp.ones((D,), jnp.float32), 'w1': jax.random.normal(ks[14], (D, F_), jnp.float32) * std, 'w2': jax.random.normal(ks[15], (F_, D), jnp.float32) * std, 'w3': jax.random.normal(ks[16], (D, F_), jnp.float32) * std}
        return inp
    _L0_attn_in = _L0_attn_setup()

    def _L0_ffn_setup():
        import jax, jax.numpy as jnp
        import numpy as np
        HIDDEN = 256
        INTER = 704
        B, S = (2, 256)

        def _ternary(key, shape):
            return jax.random.randint(key, shape, -1, 2).astype(jnp.float32)
        key = jax.random.key(seed)
        ks = jax.random.split(key, 7)
        x = jax.random.normal(ks[0], (B, S, HIDDEN), dtype=jnp.float32)
        gate_w = _ternary(ks[1], (INTER, HIDDEN))
        up_w = _ternary(ks[2], (INTER, HIDDEN))
        down_w = _ternary(ks[3], (HIDDEN, INTER))
        gate_s = jax.random.uniform(ks[4], (INTER,), minval=0.01, maxval=0.1, dtype=jnp.float32)
        up_s = jax.random.uniform(ks[5], (INTER,), minval=0.01, maxval=0.1, dtype=jnp.float32)
        down_s = jax.random.uniform(ks[6], (HIDDEN,), minval=0.01, maxval=0.1, dtype=jnp.float32)
        return {'x': x, 'gate_w': gate_w, 'up_w': up_w, 'down_w': down_w, 'gate_s': gate_s, 'up_s': up_s, 'down_s': down_s}
    _L0_ffn_in = _L0_ffn_setup()
    _d = {'L0_attn_x': _L0_attn_in['x'], 'L0_attn_norm1_w': _L0_attn_in['norm1_w'], 'L0_attn_wq': _L0_attn_in['wq'], 'L0_attn_wk': _L0_attn_in['wk'], 'L0_attn_wv': _L0_attn_in['wv'], 'L0_attn_conv_q': _L0_attn_in['conv_q'], 'L0_attn_conv_k': _L0_attn_in['conv_k'], 'L0_attn_conv_v': _L0_attn_in['conv_v'], 'L0_attn_f_a': _L0_attn_in['f_a'], 'L0_attn_f_b': _L0_attn_in['f_b'], 'L0_attn_A_log': _L0_attn_in['A_log'], 'L0_attn_dt_bias': _L0_attn_in['dt_bias'], 'L0_attn_b_w': _L0_attn_in['b_w'], 'L0_attn_g_a': _L0_attn_in['g_a'], 'L0_attn_g_b': _L0_attn_in['g_b'], 'L0_attn_onorm_w': _L0_attn_in['onorm_w'], 'L0_attn_wo': _L0_attn_in['wo'], 'L0_attn_norm2_w': _L0_attn_in['norm2_w'], 'L0_attn_w1': _L0_attn_in['w1'], 'L0_attn_w2': _L0_attn_in['w2'], 'L0_attn_w3': _L0_attn_in['w3'], 'L0_ffn_gate_w': _L0_ffn_in['gate_w'], 'L0_ffn_up_w': _L0_ffn_in['up_w'], 'L0_ffn_down_w': _L0_ffn_in['down_w'], 'L0_ffn_gate_s': _L0_ffn_in['gate_s'], 'L0_ffn_up_s': _L0_ffn_in['up_s'], 'L0_ffn_down_s': _L0_ffn_in['down_s']}
    _x0 = _d['L0_attn_x']
    _d['L0_attn_x'] = jax.random.normal(jax.random.fold_in(jax.random.key(seed), 1), (8, 256, 256), dtype=_x0.dtype)
    del _x0
    return _d

def reference(L0_attn_x, L0_attn_norm1_w, L0_attn_wq, L0_attn_wk, L0_attn_wv, L0_attn_conv_q, L0_attn_conv_k, L0_attn_conv_v, L0_attn_f_a, L0_attn_f_b, L0_attn_A_log, L0_attn_dt_bias, L0_attn_b_w, L0_attn_g_a, L0_attn_g_b, L0_attn_onorm_w, L0_attn_wo, L0_attn_norm2_w, L0_attn_w1, L0_attn_w2, L0_attn_w3, L0_ffn_gate_w, L0_ffn_up_w, L0_ffn_down_w, L0_ffn_gate_s, L0_ffn_up_s, L0_ffn_down_s):

    def _L0_attn_ref(x, norm1_w, wq, wk, wv, conv_q, conv_k, conv_v, f_a, f_b, A_log, dt_bias, b_w, g_a, g_b, onorm_w, wo, norm2_w, w1, w2, w3):
        import jax, jax.numpy as jnp
        import numpy as np
        B, S, D = (2, 256, 256)
        H, HD = (32, 128)
        P = H * HD
        K = 4
        F_ = 1024
        EPS = 1e-06

        def _rmsnorm(x, w, eps=EPS):
            xf = x.astype(jnp.float32)
            y = xf * jax.lax.rsqrt(jnp.mean(xf * xf, axis=-1, keepdims=True) + eps)
            return (y * w).astype(x.dtype)

        def _short_conv(x, w):
            k = w.shape[1]
            xp = jnp.pad(x, ((0, 0), (k - 1, 0), (0, 0)))
            y = sum((xp[:, j:j + x.shape[1], :] * w[:, j] for j in range(k)))
            return jax.nn.silu(y)

        def _l2norm(x, eps=1e-06):
            return x * jax.lax.rsqrt(jnp.sum(x * x, axis=-1, keepdims=True) + eps)

        def _kda(q, k, v, g, beta):
            scale = q.shape[-1] ** (-0.5)
            q = _l2norm(q) * scale
            k = _l2norm(k)
            tm = lambda a: jnp.swapaxes(a, 0, 1)
            qs, ks_, vs, gs, bs = (tm(q), tm(k), tm(v), tm(g), tm(beta))
            bsz, h, hd = (q.shape[0], q.shape[2], q.shape[3])
            S0 = jnp.zeros((bsz, h, hd, hd), jnp.float32)

            def step(St, inp):
                qt, kt, vt, gt, bt = inp
                St = St * jnp.exp(gt)[..., None]
                err = jnp.einsum('bhk,bhkv->bhv', kt, St)
                St = St + bt[..., None, None] * kt[..., None] * (vt - err)[..., None, :]
                ot = jnp.einsum('bhk,bhkv->bhv', qt, St)
                return (St, ot)
            _, o = jax.lax.scan(step, S0, (qs, ks_, vs, gs, bs))
            return jnp.swapaxes(o, 0, 1)
        bsz, seq, _ = x.shape
        h = _rmsnorm(x, norm1_w)
        q = _short_conv(h @ wq, conv_q).reshape(bsz, seq, H, HD)
        k = _short_conv(h @ wk, conv_k).reshape(bsz, seq, H, HD)
        v = _short_conv(h @ wv, conv_v).reshape(bsz, seq, H, HD)
        g = (h @ f_a @ f_b).reshape(bsz, seq, H, HD).astype(jnp.float32)
        g = g + dt_bias.reshape(H, HD)
        g = -jnp.exp(A_log)[:, None] * jax.nn.softplus(g)
        beta = jax.nn.sigmoid((h @ b_w).astype(jnp.float32))
        o = _kda(q.astype(jnp.float32), k.astype(jnp.float32), v.astype(jnp.float32), g, beta)
        gate = (h @ g_a @ g_b).reshape(bsz, seq, H, HD)
        og = o * jax.nn.sigmoid(gate.astype(jnp.float32))
        og = og * jax.lax.rsqrt(jnp.mean(og * og, axis=-1, keepdims=True) + EPS)
        o = (og * onorm_w).astype(x.dtype).reshape(bsz, seq, P)
        x = x + o @ wo
        h2 = _rmsnorm(x, norm2_w)
        ffn = jax.nn.silu(h2 @ w1) * (h2 @ w3) @ w2
        return x + ffn

    def _L0_ffn_ref(x, gate_w, up_w, down_w, gate_s, up_s, down_s):
        import jax, jax.numpy as jnp
        import numpy as np
        HIDDEN = 256
        INTER = 704
        B, S = (2, 256)

        def _ternary(key, shape):
            return jax.random.randint(key, shape, -1, 2).astype(jnp.float32)
        b, s, h = x.shape
        xf = x.reshape(b * s, h)
        g = jnp.einsum('th,ih->ti', xf, gate_w) * gate_s
        u = jnp.einsum('th,ih->ti', xf, up_w) * up_s
        hdn = jax.nn.silu(g) * u
        out = jnp.einsum('ti,hi->th', hdn, down_w) * down_s
        return out.reshape(b, s, -1)
    x = L0_attn_x
    x = _layernorm(x + _L0_attn_ref(x, L0_attn_norm1_w, L0_attn_wq, L0_attn_wk, L0_attn_wv, L0_attn_conv_q, L0_attn_conv_k, L0_attn_conv_v, L0_attn_f_a, L0_attn_f_b, L0_attn_A_log, L0_attn_dt_bias, L0_attn_b_w, L0_attn_g_a, L0_attn_g_b, L0_attn_onorm_w, L0_attn_wo, L0_attn_norm2_w, L0_attn_w1, L0_attn_w2, L0_attn_w3), axis=-1)
    x = _layernorm(x + _L0_ffn_ref(x, L0_ffn_gate_w, L0_ffn_up_w, L0_ffn_down_w, L0_ffn_gate_s, L0_ffn_up_s, L0_ffn_down_s), axis=-1)
    return x

_drawn_inputs = setup_inputs


def setup_inputs(seed=0):
    import zlib

    import numpy as np

    out = dict(_drawn_inputs(seed))
    spreads = {'L0_attn_norm1_w': (1.0, 0.2),
     'L0_attn_dt_bias': (0.0, 0.8),
     'L0_attn_onorm_w': (1.0, 0.2),
     'L0_attn_norm2_w': (1.0, 0.6)}
    factors = {'L0_attn_f_a': 8.0,
     'L0_attn_f_b': 8.0,
     'L0_attn_g_a': 6.688,
     'L0_attn_g_b': 6.688,
     'L0_attn_w1': 2.713,
     'L0_attn_w2': 2.685,
     'L0_attn_w3': 2.69}
    for name, (base, spread) in spreads.items():
        noise = np.random.default_rng([zlib.crc32(name.encode()), seed]).standard_normal(out[name].shape)
        drawn = base * np.exp(spread * noise) if base else spread * noise
        out[name] = jnp.asarray(drawn.astype(out[name].dtype))
    for name, factor in factors.items():
        out[name] = (out[name] * factor).astype(out[name].dtype)
    return out
```

```python
from contextlib import ExitStack

import concourse.bass as bass
from concourse import mybir

F32 = mybir.dt.float32
I32 = mybir.dt.int32
ALU = mybir.AluOpType
ACT = mybir.ActivationFunctionType

P = 128
B, S, D = 8, 256, 256
H, HD, TAPS = 32, 128, 4
FF, INTER = 1024, 704
TOK = B * S
TILES = TOK // P
KD = D // P
PAIRS = B // 2
COLS = 2 * S
CH = COLS // P
STEPS = H * PAIRS
LEVELS = 7
HALF = P // 2
EPS = 1e-6
LN_EPS = 1e-5
FK = FF // P
IK = -(-INTER // P)
BIG = 1e17
GAP, WIDE = 32, 96
GRID = 1e-11


def need(eng, sem, value):
    if not isinstance(value, int) or value > 0:
        eng.wait_ge(sem, value)


def capped(steps):
    return min(steps, STEPS) if isinstance(steps, int) else steps


def halves(ap, m, second):
    return ap.rearrange("p (r two m) -> p r two m", two=2, m=m)[:, :, second, :]


def delta_kernel(nc, ins, out):
    with ExitStack() as top:
        def sb(name, shape, dt=F32, ctx=top):
            return ctx.enter_context(nc.sbuf_tensor(name, shape, dt))

        def sem(name):
            return top.enter_context(nc.semaphore(name))

        bank = [top.enter_context(nc.psum_tensor(f"bank{i}", [P, 512], F32)) for i in range(8)]
        y_sb = sb("y_sb", [P, TILES, D])
        ident = sb("ident", [P, P])
        n2w = sb("n2w", [P, KD])
        powers = sb("powers", [P, 2, TILES])
        onorm = sb("onorm", [P, 1])

        with ExitStack() as att:
            with nc.allow_non_contiguous_dma(reason="small vectors, once"):
                attention(nc, ins, att, bank, y_sb, ident, n2w, powers, onorm)
        with ExitStack() as ffn:
            with nc.allow_non_contiguous_dma(reason="small vectors, once"):
                feed_forward(nc, ins, out, ffn, bank, y_sb, ident, n2w, powers)


def attention(nc, ins, ctx, bank, y_sb, ident, n2w, powers, onorm):
    def sb(name, shape, dt=F32):
        return ctx.enter_context(nc.sbuf_tensor(name, shape, dt))

    def sem(name):
        return ctx.enter_context(nc.semaphore(name))

    hT = sb("hT", [P, KD, TOK])
    faT = sb("faT", [P, TOK])
    gaT = sb("gaT", [P, TOK])
    masks = sb("masks", [P, LEVELS, HALF], I32)
    ones = sb("ones", [P, WIDE])
    conv_all = sb("conv_all", [P, 3, H, TAPS])
    dt_all = sb("dt_all", [P, H])
    negA_all = sb("negA_all", [P, H])
    beta_all = sb("beta_all", [P, TILES, H])
    L = sb("L", [P, LEVELS, CH * P])
    Pm = sb("Pm", [P, LEVELS, CH * P])

    with ExitStack() as pro:
        def psb(name, shape, dt=F32):
            return pro.enter_context(nc.sbuf_tensor(name, shape, dt))

        def psem(name):
            return pro.enter_context(nc.semaphore(name))

        h_tok = psb("h_tok", [P, TILES, D])
        sq = psb("sq", [P, D])
        ssq = psb("ssq", [P, TILES])
        ms = psb("ms", [P, TILES])
        rs = psb("rs", [P, TILES])
        n1w = psb("n1w", [P, KD])
        fa = psb("fa", [P, KD, HD])
        ga = psb("ga", [P, KD, HD])
        bw = psb("bw", [P, KD, H])
        beta_th = psb("beta_th", [P, CH, H])
        x_in = psem("x_in")
        w_in = psem("w_in")
        const_set = psem("const_set")
        squares_done = psem("squares_done")
        ms_done = psem("ms_done")
        rs_done = psem("rs_done")
        h_done = psem("h_done")
        hT_mm = psem("hT_mm")
        hT_done = psem("hT_done")
        low_mm = psem("low_mm")
        low_copied = psem("low_copied")
        beta_mm = psem("beta_mm")
        beta_tanh = psem("beta_tanh")
        beta_done = psem("beta_done")
        negA_exp = psem("negA_exp")
        cleared = psem("cleared")

        with nc.Block() as block:
            @block.sync
            def _(sp):
                sp.dma_start(y_sb[:, :, :], ins["L0_attn_x"].rearrange("b (c p) d -> p (b c) d", p=P)).then_inc(x_in, 16)
                sp.dma_start(ident[:, :], ins["identity"]).then_inc(w_in, 16)
                sp.dma_start(n1w[:, :], ins["L0_attn_norm1_w"].rearrange("(k p) -> p k", p=P)).then_inc(w_in, 16)
                sp.dma_start(n2w[:, :], ins["L0_attn_norm2_w"].rearrange("(k p) -> p k", p=P)).then_inc(w_in, 16)
                sp.dma_start(onorm[:, :], ins["L0_attn_onorm_w"].rearrange("(p k) -> p k", k=1)).then_inc(w_in, 16)
                sp.dma_start(fa[:, :, :], ins["L0_attn_f_a"].rearrange("(k p) r -> p k r", p=P)).then_inc(w_in, 16)
                sp.dma_start(ga[:, :, :], ins["L0_attn_g_a"].rearrange("(k p) r -> p k r", p=P)).then_inc(w_in, 16)
                sp.dma_start(bw[:, :, :], ins["L0_attn_b_w"].rearrange("(k p) r -> p k r", p=P)).then_inc(w_in, 16)
                sp.dma_start(masks[:, :, :], ins["level_masks"]).then_inc(w_in, 16)
                for i, name in enumerate(("k", "q", "v")):
                    sp.dma_start(conv_all[:, i, :, :],
                                 ins[f"L0_attn_conv_{name}"].rearrange("(h p) j -> p h j", p=P)).then_inc(w_in, 16)
                sp.dma_start(dt_all[:, :], ins["L0_attn_dt_bias"].rearrange("(h p) -> p h", p=P)).then_inc(w_in, 16)
                sp.dma_start(negA_all[:, :], ins["L0_attn_A_log"].rearrange("(o h) -> o h", o=1).to_broadcast([P, H])
                             ).then_inc(w_in, 16)
                sp.wait_ge(w_in, 16 * 13)

            @block.gpsimd
            def _(pool):
                pool.memset(powers[:, 0, :], 0.5).then_inc(const_set, 1)
                pool.memset(powers[:, 1, :], -0.5).then_inc(const_set, 1)
                pool.memset(ones[:, :], 1.0).then_inc(const_set, 1)
                pool.memset(L[:, :, :], 0.0).then_inc(cleared, 1)
                pool.wait_ge(const_set, 2)
                pool.wait_ge(ms_done, 1)
                pool.tensor_tensor(rs[:, :], ms[:, :], powers[:, 1, :], ALU.pow).then_inc(rs_done, 1)

            @block.scalar
            def _(act):
                act.wait_ge(x_in, 16)
                for i in range(TILES):
                    act.activation(sq[:, :], y_sb[:, i, :], ACT.Square, accum_out=ssq[:, i:i + 1]).then_inc(squares_done, 1)
                    act.drain()
                act.wait_ge(w_in, 16 * 13)
                act.activation(negA_all[:, :], negA_all[:, :], ACT.Exp).then_inc(negA_exp, 1)
                for g in range(PAIRS):
                    for k in range(KD):
                        act.wait_ge(hT_mm, KD * g + k + 1)
                        act.activation(hT[:, k, g * COLS:(g + 1) * COLS], bank[k][:, :], ACT.Copy,
                                       scale=n1w[:, k:k + 1]).then_inc(hT_done, 1)
                    act.wait_ge(beta_mm, g + 1)
                    act.wait_ge(beta_done, g) if g else None
                    act.activation(beta_th[:, :, :], bank[4][:, 0:CH * H].rearrange("p (n h) -> p n h", n=CH), ACT.Tanh,
                                   scale=0.5).then_inc(beta_tanh, 1)

            @block.vector
            def _(dve):
                dve.memset(Pm[:, :, :], 0.0)
                dve.wait_ge(squares_done, TILES)
                dve.tensor_scalar(ms[:, :], ssq[:, :], 1.0 / D, EPS, ALU.mult, ALU.add).then_inc(ms_done, 1)
                dve.wait_ge(negA_exp, 1)
                dve.tensor_scalar(negA_all[:, :], negA_all[:, :], -1.0, None, ALU.mult)
                dve.wait_ge(rs_done, 1)
                for i in range(TILES):
                    dve.tensor_scalar(h_tok[:, i, :], y_sb[:, i, :], rs[:, i:i + 1], None, ALU.mult).then_inc(h_done, 1)
                for g in range(PAIRS):
                    for i, dst in enumerate((faT, gaT)):
                        dve.wait_ge(low_mm, 2 * g + i + 1)
                        dve.tensor_copy(dst[:, g * COLS:(g + 1) * COLS], bank[2 + i][:, :]).then_inc(low_copied, 1)
                    dve.wait_ge(beta_tanh, g + 1)
                    dve.tensor_scalar(beta_all[:, CH * g:CH * (g + 1), :], beta_th[:, :, :], 0.5, 0.5, ALU.mult,
                                      ALU.add).then_inc(beta_done, 1)

            @block.tensor
            def _(pe):
                pe.wait_ge(w_in, 16 * 13)
                for g in range(PAIRS):
                    pe.wait_ge(h_done, CH * (g + 1))
                    for k in range(KD):
                        need(pe, hT_done, KD * (g - 1) + k + 1 if g else 0)
                        for n in range(CH):
                            mm = pe.transpose(bank[k][:, n * P:(n + 1) * P], h_tok[:, CH * g + n, k * P:(k + 1) * P],
                                              ident[:, :])
                        mm.then_inc(hT_mm, 1)
                    pe.wait_ge(hT_done, KD * (g + 1))
                    for i, w in enumerate((fa, ga)):
                        need(pe, low_copied, 2 * (g - 1) + i + 1 if g else 0)
                        for k in range(KD):
                            mm = pe.matmul(bank[2 + i][:, :], w[:, k, :], hT[:, k, g * COLS:(g + 1) * COLS],
                                           start=(k == 0), stop=(k == KD - 1))
                        mm.then_inc(low_mm, 1)
                    need(pe, beta_tanh, g)
                    for n in range(CH):
                        for k in range(KD):
                            c = g * COLS + n * P
                            mm = pe.matmul(bank[4][:, n * H:(n + 1) * H], hT[:, k, c:c + P], bw[:, k, :],
                                           start=(k == 0), stop=(k == KD - 1))
                    mm.then_inc(beta_mm, 1)

    w_qkv = sb("w_qkv", [P, 3, KD, HD])
    f_b = sb("f_b", [P, HD])
    g_b = sb("g_b", [P, HD])
    w_o = sb("w_o", [P, D])
    conv_h = sb("conv_h", [P, 3, TAPS])
    dt_h = sb("dt_h", [P, 1])
    negA_h = sb("negA_h", [P, 1])
    beta_h = sb("beta_h", [P, TILES])
    expx = sb("expx", [P, TOK])
    soft = sb("soft", [P, TOK])
    decay = sb("decay", [P, 2, COLS])
    conv = sb("conv", [P, 3, COLS])
    th = sb("th", [P, 3, COLS])
    ksuf = sb("ksuf", [P, 2, COLS])
    q_silu = sb("q_silu", [P, COLS])
    v_silu = sb("v_silu", [P, COLS])
    kq = sb("kq", [P, 4, 2, COLS])
    prods = sb("prods", [P, 3, COLS])
    totals = sb("totals", [P, COLS])
    sk4 = sb("sk4", [P, CH])
    rk = sb("rk", [P, CH])
    gamma = sb("gamma", [P, 2, CH])
    first_xp = sb("first_xp", [P, CH * HALF])
    qk_diag = sb("qk_diag", [P, CH])
    rho = sb("rho", [P, CH])
    sq_eps = sb("sq_eps", [P, 4, CH])
    X = sb("X", [P, 2, 2, CH * P])
    BT = sb("BT", [P, 4, CH * P])
    r_tok = sb("r_tok", [P, 2, CH, HD])
    r1 = sb("r1", [P, 2, HD])
    u_tok = sb("u_tok", [P, CH, HD])
    k_tok = sb("k_tok", [P, 2, HD])
    state = sb("state", [P, 2, HD])
    gate_th = sb("gate_th", [P, CH, HD])
    z_tok = sb("z_tok", [P, CH, HD])
    z_sq = sb("z_sq", [P, HD])
    z_ssq = sb("z_ssq", [P, CH])
    f_arg = sb("f_arg", [P, CH])
    f_norm = sb("f_norm", [P, CH])
    o_tok = sb("o_tok", [P, CH, HD])
    o_T = sb("o_T", [P, COLS])

    PJ, AB, PB, XB, MB = bank[0:2], bank[2:4], bank[4], bank[5], bank[6:8]

    qkv_in, fb_in, gb_in, wo_in = sem("qkv_in"), sem("fb_in"), sem("gb_in"), sem("wo_in")
    head_ready = sem("head_ready")
    g_mm, g_exp, g_x = sem("g_mm"), sem("g_exp"), sem("g_x")
    exp1_ready, ln_ready, soft_ready = sem("exp1_ready"), sem("ln_ready"), sem("soft_ready")
    proj_mm = [sem(f"{x}_mm") for x in "kqv"]
    tap3 = [sem(f"{x}_tap3") for x in "kqv"]
    conv_ready = [sem(f"{x}_conv") for x in "kqv"]
    tanh_ready = [sem(f"{x}_tanh") for x in "kqv"]
    silu_ready = [sem(f"{x}_silu") for x in "kqv"]
    decay_ready, squares_ready, qk_ready = sem("decay_ready"), sem("squares_ready"), sem("qk_ready")
    sums_mm, sums_ready, rho_ready = sem("sums_mm"), sem("sums_ready"), sem("rho_ready")
    x_init, bt_init, kq_init = sem("x_init"), sem("bt_init"), sem("kq_init")
    v_turned, r_ready = sem("v_turned"), sem("r_ready")
    ab_mm, kq_up, ks_up, total_up = sem("ab_mm"), sem("kq_up"), sem("ks_up"), sem("total_up")
    l_ready, b_ready = sem("l_ready"), sem("b_ready")
    p_mm, p_ready, x_mm, x_up = sem("p_mm"), sem("p_ready"), sem("x_mm"), sem("x_up")
    x_turned, xt_ready = sem("x_turned"), sem("xt_ready")
    gate_mm, gate_ready = sem("gate_mm"), sem("gate_ready")
    k_turned, k_ready = sem("k_turned"), sem("k_ready")
    u0_mm, u0_ready, s1_mm, s1_ready = sem("u0_mm"), sem("u0_ready"), sem("s1_mm"), sem("s1_ready")
    ks0_mm, r1_ready, u1_mm, u1_ready = sem("ks0_mm"), sem("r1_ready"), sem("u1_mm"), sem("u1_ready")
    o_mm, z_ready, ssq_ready = sem("o_mm"), sem("z_ready"), sem("ssq_ready")
    f_arg_ready, f_ready, o_ready = sem("f_arg_ready"), sem("f_ready"), sem("o_ready")
    o_turned, oT_ready, y_mm, y_added = sem("o_turned"), sem("oT_ready"), sem("y_mm"), sem("y_added")

    def chunk(n):
        return slice(n * P, (n + 1) * P)

    def ab_view(l):
        return AB[l % 2][:, :].rearrange("p (k n i) -> p k n i", k=2, n=CH)

    def total(q, l):
        if l == 0:
            return decay[:, q, :]
        n = COLS >> l
        return totals[:, COLS - 2 * n:COLS - n]

    with nc.Block() as block:
        @block.sync
        def _(sp):
            def load_fb(h):
                sp.dma_start(f_b[:, :], ins["L0_attn_f_b"][:, bass.ts(h, HD)]).then_inc(fb_in, 16)

            def load_qkv(h):
                for i, name in enumerate("kqv"):
                    sp.dma_start(w_qkv[:, i, :, :],
                                 ins[f"L0_attn_w{name}"].rearrange("(k p) c -> p k c", p=P)[:, :, bass.ts(h, HD)]
                                 ).then_inc(qkv_in, 16)

            def load_gb(h):
                sp.dma_start(g_b[:, :], ins["L0_attn_g_b"][:, bass.ts(h, HD)]).then_inc(gb_in, 16)

            def load_wo(h):
                sp.dma_start(w_o[:, :], ins["L0_attn_wo"][bass.ts(h, HD), :]).then_inc(wo_in, 16)

            load_fb(0)
            load_qkv(0)
            load_gb(0)
            load_wo(0)
            with sp.Fori(1, H) as h:
                sp.wait_ge(g_mm, PAIRS * h)
                load_fb(h)
                sp.wait_ge(proj_mm[2], PAIRS * h)
                load_qkv(h)
                sp.wait_ge(gate_mm, PAIRS * h)
                load_gb(h)
                sp.wait_ge(y_mm, 2 * PAIRS * h)
                load_wo(h)
            sp.wait_ge(qkv_in, 48 * H)

        @block.tensor
        def _(pe):
            def decay_projection(g, k, t):
                b = (k + 1) % 2
                if k == 0:
                    pe.wait_ge(fb_in, 16 * (g + 1))
                    need(pe, conv_ready[1], t + 2)
                elif k == 1:
                    need(pe, conv_ready[2], t + 2)
                else:
                    pe.wait_ge(g_x, PAIRS * g + k - 1)
                pe.matmul(PJ[b][:, :], f_b[:, :], faT[:, k * COLS:(k + 1) * COLS], start=True, stop=True
                          ).then_inc(g_mm, 1)

            def project(i, t, j, g):
                s, pair = t + 1, (j + 1) % 4
                if i == 0:
                    if j == 3:
                        pe.wait_ge(qkv_in, 48 * (g + 1))
                        pe.wait_ge(g_x, PAIRS * (g + 1))
                    need(pe, conv_ready[2], s)
                elif i == 1:
                    if j == 3:
                        pe.wait_ge(g_x, PAIRS * (g + 1) - 1)
                    need(pe, gate_ready, t)
                else:
                    pe.wait_ge(conv_ready[0], s + 1)
                for k in range(KD):
                    mm = pe.matmul(PJ[i % 2][:, :], w_qkv[:, i, k, :], hT[:, k, pair * COLS:(pair + 1) * COLS],
                                   start=(k == 0), stop=(k == KD - 1))
                mm.then_inc(proj_mm[i], 1)

            def sums(t):
                s = t + 1
                pe.wait_ge(squares_ready, s + 1)
                pe.wait_ge(qk_ready, s + 1)
                need(pe, y_added, 2 * (t - 1))
                for a in range(3):
                    for n in range(CH):
                        c = GAP * (CH * a + n)
                        mm = pe.matmul(MB[1][:, c:c + WIDE], prods[:, a, chunk(n)], ones[:, :], start=True, stop=True)
                mm.then_inc(sums_mm, 1)

            def turn_v(t):
                pe.wait_ge(silu_ready[2], t + 2)
                pe.wait_ge(sums_ready, t + 2)
                for n in range(CH):
                    mm = pe.transpose(MB[1][:, chunk(n)], v_silu[:, chunk(n)], ident[:, :])
                mm.then_inc(v_turned, 1)

            def pairs_level(l, t, q, j):
                m = 1 << l
                if l == 0:
                    pe.wait_ge(kq_init, t + 1)
                    need(pe, b_ready, 7 * t)
                else:
                    pe.wait_ge(kq_up, 7 * t + l)
                    pe.wait_ge(ks_up, 7 * t + l)
                    need(pe, b_ready, 7 * t + l - 1)
                for n in range(CH):
                    rhs = kq[:, j, :, chunk(n)].rearrange("p k (r two m) -> p k r two m", two=2, m=m)[:, :, :, 1, :]
                    mm = pe.matmul(ab_view(l)[:, :, n, :], ksuf[:, q, chunk(n)], rhs, start=True, stop=True)
                mm.then_inc(ab_mm, 1)

            def inverse_p(l, t, q):
                pe.wait_ge(l_ready, 7 * t + l + 1)
                if l == 0:
                    pe.wait_ge(x_init, t + 1)
                    need(pe, p_ready, 6 * t)
                else:
                    pe.wait_ge(x_up, 7 * t + l)
                for n in range(CH):
                    mm = pe.matmul(PB[:, chunk(n)], L[:, l, chunk(n)], X[:, q, 0, chunk(n)], start=True, stop=True)
                mm.then_inc(p_mm, 1)

            def inverse_x(l, t, q):
                pe.wait_ge(p_ready, 6 * t + l)
                pe.wait_ge(xt_ready, 6 * t + l)
                for n in range(CH):
                    if l < LEVELS - 1:
                        mm = pe.matmul(XB[:, chunk(n)], X[:, q, 1, chunk(n)], Pm[:, l, chunk(n)], start=True, stop=True)
                    else:
                        mm = pe.matmul(XB[:, chunk(n)], Pm[:, l, chunk(n)], X[:, q, 1, chunk(n)], start=True, stop=True)
                mm.then_inc(x_mm, 1)

            def turn_x(l, t, q):
                pe.wait_ge(x_up, 7 * t + l + 1)
                for n in range(CH):
                    mm = pe.transpose(XB[:, chunk(n)], X[:, q, 0, chunk(n)], ident[:, :])
                mm.then_inc(x_turned, 1)

            def gate(t, j, hd):
                pair = (j - 1) % 4
                if j == 1:
                    pe.wait_ge(gb_in, 16 * (hd + 1))
                if j == 3:
                    need(pe, g_x, capped(PAIRS * (hd + 2) - 1))
                pe.wait_ge(conv_ready[1], capped(t + 1))
                for n in range(CH):
                    c = pair * COLS + n * P
                    mm = pe.matmul(PJ[1][:, chunk(n)], gaT[:, c:c + P], g_b[:, :], start=True, stop=True)
                mm.then_inc(gate_mm, 1)

            def turn_k(t, q):
                pe.wait_ge(ks_up, 7 * t)
                pe.wait_ge(r_ready, capped(t + 1))
                for b in range(2):
                    mm = pe.transpose(MB[1][:, chunk(b)], ksuf[:, q, chunk(2 * b)], ident[:, :])
                mm.then_inc(k_turned, 1)

            def first_u(t, q):
                pe.wait_ge(x_up, 7 * t)
                pe.wait_ge(r_ready, t)
                need(pe, z_ready, t - 1)
                for b in range(2):
                    mm = pe.matmul(MB[0][:, chunk(b)], X[:, q, 1, chunk(2 * b)], r_tok[:, q, 2 * b, :],
                                   start=True, stop=True)
                mm.then_inc(u0_mm, 1)

            def first_state(t):
                pe.wait_ge(k_ready, t)
                pe.wait_ge(u0_ready, t)
                for b in range(2):
                    mm = pe.matmul(MB[0][:, chunk(b)], k_tok[:, b, :], u_tok[:, 2 * b, :], start=True, stop=True)
                mm.then_inc(s1_mm, 1)

            def state_k(t, j):
                pe.wait_ge(s1_ready, t)
                pe.wait_ge(kq_up, 7 * t)
                for b in range(2):
                    mm = pe.matmul(MB[0][:, chunk(b)], kq[:, (j - 1) % 4, 0, chunk(2 * b + 1)], state[:, b, :],
                                   start=True, stop=True)
                mm.then_inc(ks0_mm, 1)

            def second_u(t, q):
                pe.wait_ge(r1_ready, t)
                for b in range(2):
                    mm = pe.matmul(MB[0][:, chunk(b)], X[:, q, 1, chunk(2 * b + 1)], r1[:, b, :], start=True, stop=True)
                mm.then_inc(u1_mm, 1)

            def outputs(t, j):
                last = (j - 1) % 4
                pe.wait_ge(u1_ready, t)
                pe.wait_ge(b_ready, 7 * t)
                for n in range(CH):
                    mm = pe.matmul(MB[0][:, chunk(n)], BT[:, last, chunk(n)], u_tok[:, n, :], start=True, stop=(n % 2 == 0))
                    if n % 2:
                        mm = pe.matmul(MB[0][:, chunk(n)], kq[:, last, 1, chunk(n)], state[:, n // 2, :],
                                       start=False, stop=True)
                mm.then_inc(o_mm, 1)

            def turn_o(t):
                pe.wait_ge(o_ready, t - 1)
                pe.wait_ge(k_ready, capped(t))
                for n in range(CH):
                    mm = pe.transpose(MB[1][:, chunk(n)], o_tok[:, n, :], ident[:, :])
                mm.then_inc(o_turned, 1)

            def output_product(t, j, hd, i):
                if i == 0:
                    if j == 2:
                        pe.wait_ge(wo_in, 16 * (hd + 1))
                    pe.wait_ge(oT_ready, t - 1)
                else:
                    pe.wait_ge(y_added, 2 * (t - 2) + 1)
                for n in range(2):
                    mm = pe.matmul(MB[1][:, n * D:(n + 1) * D], o_T[:, chunk(2 * i + n)], w_o[:, :],
                                   start=True, stop=True)
                mm.then_inc(y_mm, 1)

            def slot(t, j, hd, front=False, middle=False, back=False, outp=False, ahead=False):
                q, o = j % 2, (j + 1) % 2
                g = hd + 1
                if middle:
                    pairs_level(0, t, q, j)
                if back:
                    inverse_p(6, t - 1, o)
                    turn_x(5, t - 1, o)
                    gate(t, j, hd)
                    inverse_x(6, t - 1, o)
                if middle:
                    pairs_level(1, t, q, j)
                if back:
                    turn_k(t, o)
                if front:
                    project(0, t, j, g)
                if middle:
                    inverse_p(0, t, q)
                    pairs_level(2, t, q, j)
                if back:
                    first_u(t, o)
                if middle:
                    inverse_p(1, t, q)
                    turn_x(0, t, q)
                if front:
                    project(1, t, j, g)
                if outp:
                    turn_o(t)
                if middle:
                    inverse_x(1, t, q)
                    pairs_level(3, t, q, j)
                if back:
                    first_state(t)
                if front:
                    project(2, t, j, g)
                if middle:
                    inverse_p(2, t, q)
                    turn_x(1, t, q)
                if outp:
                    output_product(t, j, hd, 0)
                if middle:
                    inverse_x(2, t, q)
                    pairs_level(4, t, q, j)
                if back:
                    state_k(t, j)
                if middle:
                    inverse_p(3, t, q)
                    turn_x(2, t, q)
                if outp:
                    output_product(t, j, hd, 1)
                if ahead:
                    decay_projection(g, 0, t)
                    decay_projection(g, 1, t)
                if middle:
                    inverse_x(3, t, q)
                    pairs_level(5, t, q, j)
                if back:
                    second_u(t, o)
                if middle:
                    inverse_p(4, t, q)
                    turn_x(3, t, q)
                if ahead:
                    decay_projection(g, 2, t)
                    decay_projection(g, 3, t)
                if front:
                    sums(t)
                if middle:
                    inverse_x(4, t, q)
                    pairs_level(6, t, q, j)
                if back:
                    outputs(t, j)
                if middle:
                    inverse_p(5, t, q)
                    turn_x(4, t, q)
                if front:
                    turn_v(t)
                if middle:
                    inverse_x(5, t, q)

            for k in range(PAIRS):
                decay_projection(0, k, -2)
            run_slots(pe, slot)

        @block.scalar
        def _(act):
            def decay_exp(g, k):
                act.wait_ge(g_x, PAIRS * g + k + 1)
                if k == 0:
                    need(act, soft_ready, g)
                act.activation(expx[:, k * COLS:(k + 1) * COLS], soft[:, k * COLS:(k + 1) * COLS], ACT.Exp
                               ).then_inc(g_exp, 1)

            def decay_ln(g):
                act.wait_ge(exp1_ready, g + 1)
                act.activation(expx[:, :], expx[:, :], ACT.Ln).then_inc(ln_ready, 1)

            def decay_of_step(t, j, g):
                pair, o = (j + 1) % 4, (j + 1) % 2
                if j == 3:
                    act.wait_ge(soft_ready, g + 1)
                    act.wait_ge(head_ready, g + 1)
                need(act, kq_init, t)
                need(act, kq_up, 7 * (t - 1) + 1)
                need(act, ks_up, 7 * (t - 1) + 1)
                act.activation(decay[:, o, :], soft[:, pair * COLS:(pair + 1) * COLS], ACT.Exp,
                               scale=negA_h[:, :]).then_inc(decay_ready, 1)

            def last_tap(i, t, j, g):
                act.wait_ge(proj_mm[i], t + 2)
                need(act, silu_ready[i], t + 1)
                if i == 0 and j == 3:
                    act.wait_ge(head_ready, g + 1)
                act.activation(conv[:, i, :], PJ[i % 2][:, :], ACT.Copy, scale=conv_h[:, i, TAPS - 1:TAPS]
                               ).then_inc(tap3[i], 1)

            def tanh(i, t):
                act.wait_ge(conv_ready[i], t + 2)
                act.activation(th[:, i, :], conv[:, i, :], ACT.Tanh, scale=0.5).then_inc(tanh_ready[i], 1)

            def squares(t):
                act.wait_ge(silu_ready[0], t + 2)
                act.wait_ge(silu_ready[1], t + 2)
                need(act, sums_mm, t + 1)
                act.activation(prods[:, 0, :], ksuf[:, squares.o, :], ACT.Square)
                act.activation(prods[:, 1, :], q_silu[:, :], ACT.Square).then_inc(squares_ready, 1)

            def transposed_x(l, t, q):
                act.wait_ge(x_turned, 6 * t + l + 1)
                new = (lambda ap: halves(ap, 1 << l, 1)) if l else (lambda ap: ap)
                act.activation(new(X[:, q, 1, :]), new(XB[:, :]), ACT.Copy).then_inc(xt_ready, 1)

            def minus_p(l, t):
                act.wait_ge(p_mm, 7 * t + l + 1)
                act.activation(halves(Pm[:, l, :], 1 << l, 0), halves(PB[:, :], 1 << l, 0), ACT.Copy, scale=-1.0
                               ).then_inc(p_ready, 1)

            def slot(t, j, hd, front=False, middle=False, back=False, outp=False, ahead=False):
                q, o = j % 2, (j + 1) % 2
                g = hd + 1
                if front:
                    decay_of_step(t, j, g)
                if back:
                    minus_p(6, t - 1)
                    transposed_x(5, t - 1, o)
                    act.wait_ge(gate_mm, t)
                    need(act, z_ready, t - 1)
                    act.activation(gate_th[:, :, :], PJ[1][:, :].rearrange("p (n v) -> p n v", n=CH), ACT.Tanh,
                                   scale=0.5).then_inc(gate_ready, 1)
                    act.wait_ge(k_turned, t)
                    need(act, s1_mm, t - 1)
                    act.activation(k_tok[:, :, :], MB[1][:, 0:2 * P].rearrange("p (b d) -> p b d", b=2), ACT.Copy
                                   ).then_inc(k_ready, 1)
                if front:
                    last_tap(0, t, j, g)
                if back:
                    act.wait_ge(u0_mm, t)
                    need(act, o_mm, t - 1)
                    act.activation(u_tok[:, 0:CH:2, :], MB[0][:, 0:2 * P].rearrange("p (b d) -> p b d", b=2), ACT.Copy
                                   ).then_inc(u0_ready, 1)
                if middle:
                    minus_p(1, t)
                    transposed_x(0, t, q)
                if front:
                    tanh(0, t)
                    last_tap(1, t, j, g)
                if outp:
                    act.wait_ge(o_turned, t - 1)
                    act.activation(o_T[:, :], MB[1][:, :], ACT.Copy, scale=onorm[:, :]).then_inc(oT_ready, 1)
                if back:
                    act.wait_ge(s1_mm, t)
                    act.activation(state[:, :, :], MB[0][:, 0:2 * P].rearrange("p (b d) -> p b d", b=2), ACT.Copy
                                   ).then_inc(s1_ready, 1)
                if front:
                    tanh(1, t)
                    last_tap(2, t, j, g)
                if middle:
                    minus_p(2, t)
                    transposed_x(1, t, q)
                if front:
                    squares.o = o
                    squares(t)
                if middle:
                    minus_p(3, t)
                    transposed_x(2, t, q)
                if front:
                    tanh(2, t)
                if ahead:
                    decay_exp(g, 0)
                    decay_exp(g, 1)
                if back:
                    act.wait_ge(u1_mm, t)
                    act.activation(u_tok[:, 1:CH:2, :], MB[0][:, 0:2 * P].rearrange("p (b d) -> p b d", b=2), ACT.Copy
                                   ).then_inc(u1_ready, 1)
                if middle:
                    minus_p(4, t)
                    transposed_x(3, t, q)
                if ahead:
                    decay_exp(g, 2)
                    decay_exp(g, 3)
                if middle:
                    minus_p(5, t)
                    transposed_x(4, t, q)
                if back:
                    act.wait_ge(z_ready, t)
                    need(act, f_arg_ready, t - 1)
                    for n in range(CH):
                        sq = act.activation(z_sq[:, :], z_tok[:, n, :], ACT.Square, accum_out=z_ssq[:, n:n + 1])
                        if n == CH - 1:
                            sq.then_inc(ssq_ready, 1)
                        act.drain()
                if ahead:
                    decay_ln(g)

            for k in range(PAIRS):
                decay_exp(0, k)
            decay_ln(0)
            run_slots(act, slot)

        @block.vector
        def _(dve):
            def decay_bias(g):
                dve.tensor_copy(dt_h[:, :], dt_all[:, bass.ds(g, 1)])
                dve.drain()

            def decay_x(g, k):
                b = (k + 1) % 2
                dve.wait_ge(g_mm, PAIRS * g + k + 1)
                need(dve, decay_ready, PAIRS * (g - 1) + k + 1)
                dve.tensor_scalar(soft[:, k * COLS:(k + 1) * COLS], PJ[b][:, :], dt_h[:, :], None, ALU.add
                                  ).then_inc(g_x, 1)

            def decay_exp1(g):
                dve.wait_ge(g_exp, PAIRS * (g + 1))
                dve.tensor_scalar(expx[:, :], expx[:, :], BIG, 1.0, ALU.min, ALU.add).then_inc(exp1_ready, 1)

            def decay_soft(g):
                dve.wait_ge(ln_ready, g + 1)
                need(dve, decay_ready, PAIRS * g)
                dve.tensor_tensor(soft[:, :], soft[:, :], expx[:, :], ALU.max).then_inc(soft_ready, 1)

            def head_scalars(g):
                need(dve, decay_ready, PAIRS * g)
                need(dve, tap3[2], PAIRS * g)
                dve.tensor_copy(negA_h[:, :], negA_all[:, bass.ds(g, 1)])
                dve.tensor_copy(beta_h[:, :].unsqueeze(2), beta_all[:, :, bass.ds(g, 1)])
                dve.tensor_copy(conv_h[:, :, :].unsqueeze(2), conv_all[:, :, bass.ds(g, 1), :]).then_inc(head_ready, 1)
                dve.drain()

            def taps(i, t, backs=range(1, TAPS)):
                if backs[0] == 1:
                    dve.wait_ge(tap3[i], t + 2)
                acc = conv[:, i, :].rearrange("p (b s) -> p b s", b=2)
                src = PJ[i % 2][:, :].rearrange("p (b s) -> p b s", b=2)
                for back in backs:
                    w = conv_h[:, i, TAPS - 1 - back:TAPS - back]
                    op = dve.scalar_tensor_tensor(out=acc[:, :, back:], in0=src[:, :, :S - back], scalar=w,
                                                  in1=acc[:, :, back:], op0=ALU.mult, op1=ALU.add)
                    if back < TAPS - 1:
                        dve.drain()
                    else:
                        op.then_inc(conv_ready[i], 1)

            def silu(i, t, dst):
                dve.wait_ge(tanh_ready[i], t + 2)
                if i == 0:
                    need(dve, k_turned, t)
                if i == 1:
                    need(dve, squares_ready, t + 1)
                    need(dve, qk_ready, t + 1)
                if i == 2:
                    need(dve, v_turned, t + 1)
                dve.scalar_tensor_tensor(out=dst, in0=th[:, i, :], scalar=1.0, in1=conv[:, i, :], op0=ALU.add,
                                         op1=ALU.mult).then_inc(silu_ready[i], 1)

            def norms(t, j):
                pair = (j + 1) % 4
                dve.wait_ge(sums_mm, t + 2)
                need(dve, rho_ready, t + 1)
                need(dve, bt_init, t + 1)
                need(dve, x_init, t + 1)
                kk, qq, qk = (MB[1][:, GAP * CH * a:GAP * CH * (a + 1)].rearrange("p (n g) -> p n g", g=GAP)[:, :, 0]
                              for a in range(3))
                dve.tensor_scalar(sk4[:, :], kk, 4 * EPS, 0.25, ALU.add, ALU.mult)
                dve.tensor_scalar(rk[:, :], kk, 4 * EPS, None, ALU.add)
                dve.tensor_scalar(sq_eps[:, pair, :], qq, 4 * EPS, 4 * HD * EPS, ALU.add, ALU.mult)
                dve.tensor_copy(qk_diag[:, :], qk)
                dve.drain()
                dve.reciprocal(rk[:, :], rk[:, :])
                dve.drain()
                dve.tensor_tensor(gamma[:, (j + 1) % 2, :], rk[:, :], beta_h[:, CH * pair:CH * (pair + 1)], ALU.mult
                                  ).then_inc(sums_ready, 1)

            def scaled_v(t, o):
                dve.wait_ge(v_turned, t + 2)
                dve.wait_ge(rho_ready, t + 2)
                need(dve, u0_mm, t)
                dve.tensor_tensor(r_tok[:, o, :, :], MB[1][:, :].rearrange("p (n v) -> p n v", n=CH),
                                  rho[:, :].unsqueeze(2).to_broadcast([P, CH, HD]), ALU.mult).then_inc(r_ready, 1)

            def first_kq(t, j, o):
                b = (j + 1) % 4
                dve.wait_ge(decay_ready, t + 2)
                dve.wait_ge(silu_ready[1], t + 2)
                dve.tensor_tensor(kq[:, b, 0, :], ksuf[:, o, :], decay[:, o, :], ALU.mult)
                dve.tensor_tensor(kq[:, b, 1, :], q_silu[:, :], decay[:, o, :], ALU.mult)
                dve.drain()

            def round_kq(j):
                b = (j + 1) % 4
                dve.tensor_scalar(kq[:, b, :, :], kq[:, b, :, :], GRID, -GRID, ALU.add, ALU.add).then_inc(kq_init, 1)

            def level(l, t, q, j):
                m = 1 << l
                dve.wait_ge(ab_mm, 7 * t + l + 1)
                if l:
                    dve.wait_ge(total_up, 6 * t + l)
                    dve.wait_ge(b_ready, 7 * t + l)
                else:
                    dve.wait_ge(bt_init, t + 1)
                need(dve, p_mm, 7 * (t - 1) + l + 1)
                step = 2 if l == LEVELS - 1 else 1
                view = kq[:, j, :, :].rearrange("p k (r two m) -> p k r two m", two=2, m=m)[:, :, step - 1::step, 1, :]
                tot = total(q, l).rearrange("p (r two) -> p r two", two=2)[:, step - 1::step, 0]
                r = tot.shape[1]
                dve.tensor_tensor(view, view, tot.unsqueeze(1).unsqueeze(3).to_broadcast([P, 2, r, m]), ALU.mult)
                dve.drain()
                dve.tensor_scalar(view, view, GRID, -GRID, ALU.add, ALU.add).then_inc(kq_up, 1)
                mask = masks[:, l, :].rearrange("p (r m) -> p r m", m=m).unsqueeze(1).to_broadcast([P, CH, HALF // m, m])
                for i, dst, done in ((0, L[:, l, :], l_ready), (1, BT[:, j, :], b_ready)):
                    out = dst.rearrange("p (n r two m) -> p n r two m", n=CH, two=2, m=m)[:, :, :, 1, :]
                    src = ab_view(l)[:, i, :, :].rearrange("p n (r m) -> p n r m", m=m)
                    dve.copy_predicated(out, mask, src).then_inc(done, 1)

            def x_update(l, t, q):
                m = 1 << l
                if l == 0:
                    dve.wait_ge(p_mm, 7 * t + 1)
                    xp = first_xp[:, :].rearrange("p (n i) -> p n i", n=CH)
                    dve.tensor_tensor(xp, halves(PB[:, :], 1, 0)[:, :, 0].rearrange("p (n i) -> p n i", n=CH),
                                      gamma[:, q, :].unsqueeze(2).to_broadcast([P, CH, HALF]), ALU.mult)
                    dve.drain()
                    x = halves(X[:, q, 0, :], 1, 0)
                    dve.tensor_tensor(x, x, first_xp[:, :].unsqueeze(2), ALU.subtract).then_inc(x_up, 1)
                    return
                dve.wait_ge(x_mm, 6 * t + l)
                w, second = (0, 0) if l < LEVELS - 1 else (1, 1)
                x = halves(X[:, q, w, :], m, second)
                dve.tensor_tensor(x, halves(XB[:, :], m, second), x, ALU.add).then_inc(x_up, 1)

            def y_add(t, j, i):
                tile = CH * ((j - 2) % 4) + 2 * i
                dve.wait_ge(y_mm, 2 * (t - 2) + i + 1)
                y = y_sb[:, tile:tile + 2, :]
                dve.tensor_tensor(y, MB[1][:, :].rearrange("p (n d) -> p n d", n=2), y, ALU.add).then_inc(y_added, 1)

            def slot(t, j, hd, front=False, middle=False, back=False, outp=False, ahead=False):
                q, o = j % 2, (j + 1) % 2
                g = hd + 1
                if front and j == 3:
                    head_scalars(g)
                if ahead:
                    decay_bias(g)
                if middle:
                    level(0, t, q, j)
                if outp:
                    dve.wait_ge(ssq_ready, t - 1)
                    dve.scalar_tensor_tensor(out=f_arg[:, :], in0=z_ssq[:, :], scalar=1.0 / HD,
                                             in1=sq_eps[:, (j - 2) % 4, :], op0=ALU.mult, op1=ALU.add
                                             ).then_inc(f_arg_ready, 1)
                if back:
                    x_update(6, t - 1, o)
                if middle:
                    level(1, t, q, j)
                    x_update(0, t, q)
                if front:
                    taps(0, t)
                if outp:
                    dve.wait_ge(f_ready, t - 1)
                    dve.tensor_tensor(o_tok[:, :, :], z_tok[:, :, :],
                                      f_norm[:, :].unsqueeze(2).to_broadcast([P, CH, HD]), ALU.mult).then_inc(o_ready, 1)
                if middle:
                    level(2, t, q, j)
                if front:
                    silu(0, t, ksuf[:, o, :])
                    taps(1, t, range(1, TAPS - 1))
                if middle:
                    x_update(1, t, q)
                if front:
                    taps(1, t, range(TAPS - 1, TAPS))
                if middle:
                    level(3, t, q, j)
                if front:
                    silu(1, t, q_silu[:, :])
                    first_kq(t, j, o)
                if middle:
                    x_update(2, t, q)
                if front:
                    round_kq(j)
                if outp:
                    y_add(t, j, 0)
                if middle:
                    level(4, t, q, j)
                if back:
                    dve.wait_ge(ks0_mm, t)
                    dve.tensor_tensor(r1[:, :, :], r_tok[:, o, 1:CH:2, :],
                                      MB[0][:, 0:2 * P].rearrange("p (b d) -> p b d", b=2), ALU.subtract
                                      ).then_inc(r1_ready, 1)
                if front:
                    taps(2, t, range(1, TAPS if ahead else TAPS - 1))
                if ahead:
                    decay_x(g, 0)
                    decay_x(g, 1)
                if middle:
                    x_update(3, t, q)
                if front and not ahead:
                    taps(2, t, range(TAPS - 1, TAPS))
                if outp:
                    y_add(t, j, 1)
                if middle:
                    level(5, t, q, j)
                if front:
                    silu(2, t, v_silu[:, :])
                if ahead:
                    decay_x(g, 2)
                    decay_x(g, 3)
                    decay_exp1(g)
                if front:
                    norms(t, j)
                if middle:
                    x_update(4, t, q)
                    level(6, t, q, j)
                if back:
                    dve.wait_ge(o_mm, t)
                    dve.wait_ge(gate_ready, t)
                    need(dve, ssq_ready, t - 1)
                    dve.scalar_tensor_tensor(out=z_tok[:, :, :], in0=gate_th[:, :, :], scalar=1.0,
                                             in1=MB[0][:, :].rearrange("p (n v) -> p n v", n=CH), op0=ALU.add,
                                             op1=ALU.mult).then_inc(z_ready, 1)
                if front:
                    scaled_v(t, o)
                if middle:
                    x_update(5, t, q)
                if ahead:
                    decay_soft(g)

            decay_bias(0)
            for k in range(PAIRS):
                decay_x(0, k)
            decay_exp1(0)
            decay_soft(0)
            run_slots(dve, slot)

        @block.gpsimd
        def _(pool):
            def level(l, t, q):
                m = 1 << l
                pool.wait_ge(ab_mm, 7 * t + l + 1)
                if l == 0:
                    pool.wait_ge(kq_init, t + 1)
                tot = total(q, l).rearrange("p (r two) -> p r two", two=2)
                if l < LEVELS - 1:
                    if l:
                        pool.wait_ge(total_up, 6 * t + l)
                    pool.tensor_tensor(total(q, l + 1), tot[:, :, 0], tot[:, :, 1], ALU.mult).then_inc(total_up, 1)
                step = 2 if l == LEVELS - 1 else 1
                view = ksuf[:, q, :].rearrange("p (r two m) -> p r two m", two=2, m=m)[:, 0::step, 0, :]
                tot = tot[:, 0::step, 1]
                pool.tensor_tensor(view, view, tot.unsqueeze(2).to_broadcast([P, tot.shape[1], m]), ALU.mult)
                pool.drain()
                pool.tensor_scalar(view, view, GRID, -GRID, ALU.add, ALU.add).then_inc(ks_up, 1)

            def wide(cols):
                return cols.unsqueeze(2).to_broadcast([P, CH, P])

            def slot(t, j, hd, front=False, middle=False, back=False, outp=False, ahead=False):
                q, o = j % 2, (j + 1) % 2
                eye = ident[:, :].unsqueeze(1).to_broadcast([P, CH, P])
                if middle:
                    level(0, t, q)
                if outp:
                    pool.wait_ge(f_arg_ready, t - 1)
                    pool.tensor_tensor(f_norm[:, :], f_arg[:, :], powers[:, 1, 0:CH], ALU.pow).then_inc(f_ready, 1)
                if middle:
                    level(1, t, q)
                    level(2, t, q)
                    level(3, t, q)
                if front:
                    pool.wait_ge(silu_ready[0], t + 2)
                    pool.wait_ge(silu_ready[1], t + 2)
                    need(pool, sums_mm, t + 1)
                    pool.tensor_tensor(prods[:, 2, :], ksuf[:, o, :], q_silu[:, :], ALU.mult).then_inc(qk_ready, 1)
                if middle:
                    level(4, t, q)
                    level(5, t, q)
                if front:
                    pool.wait_ge(sums_ready, t + 2)
                    need(pool, r_ready, t + 1)
                    pool.tensor_tensor(rho[:, :], sk4[:, :], powers[:, 0, 0:CH], ALU.pow).then_inc(rho_ready, 1)
                    pool.tensor_tensor(BT[:, (j + 1) % 4, :].rearrange("p (n i) -> p n i", n=CH), eye,
                                       wide(qk_diag[:, :]), ALU.mult).then_inc(bt_init, 1)
                if middle:
                    level(6, t, q)
                if front:
                    need(pool, u1_mm, t)
                    pool.tensor_tensor(X[:, o, 0, :].rearrange("p (n i) -> p n i", n=CH), eye, wide(gamma[:, o, :]),
                                       ALU.mult).then_inc(x_init, 1)

            run_slots(pool, slot)


def run_slots(eng, slot):
    full = dict(front=True, middle=True, back=True, outp=True)
    slot(-1, 3, -1, front=True)
    slot(0, 0, 0, front=True, middle=True)
    slot(1, 1, 0, front=True, middle=True, back=True)
    with eng.Fori(0, H - 1) as h:
        for i in range(PAIRS):
            slot(PAIRS * h + 2 + i, (2 + i) % PAIRS, h + (2 + i) // PAIRS, ahead=(i == 0), **full)
    slot(STEPS - 2, 2, H - 1, **full)
    slot(STEPS - 1, 3, H - 1, middle=True, back=True, outp=True)
    slot(STEPS, 0, H, back=True, outp=True)
    slot(STEPS + 1, 1, H, outp=True)


def feed_forward(nc, ins, out, ctx, bank, y_sb, ident, n2w, powers):
    def sb(name, shape, dt=F32):
        return ctx.enter_context(nc.sbuf_tensor(name, shape, dt))

    def sem(name):
        return ctx.enter_context(nc.semaphore(name))

    LASTI = INTER - (IK - 1) * P
    w1 = sb("w1", [P, KD, FF])
    w3 = sb("w3", [P, KD, FF])
    w2 = sb("w2", [P, FK, D])
    raw = sb("raw", [P, 2, IK, D])
    down_raw = sb("down_raw", [P, KD, INTER])
    gate_T = sb("gate_T", [P, 2, KD, INTER])
    down_T = sb("down_T", [P, IK, D])
    sc = sb("sc", [P, 2, IK])
    half_s = sb("half_s", [P, 2, IK])
    down_s = sb("down_s", [P, KD])
    xin = sb("xin", [P, CH, D])
    sq = sb("f_sq", [P, D])
    ssq = sb("f_ssq", [P, CH])
    ms = sb("f_ms", [P, CH])
    rs = sb("f_rs", [P, CH])
    h2 = sb("h2", [P, CH, D])
    hT = sb("f_hT", [P, KD, COLS])
    th = sb("f_th", [P, 2, COLS])
    t1 = sb("f_t1", [P, 2, COLS])
    gT = sb("gT", [P, FK, COLS])
    res = sb("res", [P, CH, D])
    stats = sb("stats", [P, CH, 6])
    mv = sb("mv", [P, CH, 2])
    var = sb("var", [P, CH])
    rstd = sb("rstd", [P, CH])
    x2 = sb("x2", [P, CH, D])
    fin = sb("fin", [P, CH, D])

    w_in, x_in, out_done = sem("f_w_in"), sem("f_x_in"), sem("out_done")
    w_turned, w_copied, scales_ready = sem("w_turned"), sem("w_copied"), sem("scales_ready")
    ssq_done, ms_done, rs_done, h2_done = sem("f_ssq_done"), sem("f_ms_done"), sem("f_rs_done"), sem("f_h2_done")
    turned, hT_done = sem("f_turned"), sem("f_hT_done")
    up_mm, tanh_done, gated = sem("up_mm"), sem("f_tanh_done"), sem("gated")
    down_mm, res_done = sem("down_mm"), sem("res_done")
    var_done, rstd_done, ln_done = sem("var_done"), sem("rstd_done"), sem("ln_done")
    UNITS = FK + IK

    def rows(i):
        return P if i < IK - 1 else LASTI

    xr = ins["L0_attn_x"].rearrange("b (c p) d -> p (b c) d", p=P)
    outr = out.rearrange("b (c p) d -> p (b c) d", p=P)

    with nc.Block() as block:
        @block.sync
        def _(sp):
            sp.dma_start(w1[:, :, :], ins["L0_attn_w1"].rearrange("(k p) f -> p k f", p=P)).then_inc(w_in, 16)
            sp.dma_start(w3[:, :, :], ins["L0_attn_w3"].rearrange("(k p) f -> p k f", p=P)).then_inc(w_in, 16)
            sp.dma_start(w2[:, :, :], ins["L0_attn_w2"].rearrange("(k p) f -> p k f", p=P)).then_inc(w_in, 16)
            full = (IK - 1) * P
            for i, name in enumerate(("gate", "up")):
                w = ins[f"L0_ffn_{name}_w"]
                s = ins[f"L0_ffn_{name}_s"]
                sp.dma_start(raw[:, i, 0:IK - 1, :], w[0:full, :].rearrange("(k p) f -> p k f", p=P)).then_inc(w_in, 16)
                sp.dma_start(raw[0:LASTI, i, IK - 1, :], w[full:INTER, :]).then_inc(w_in, 16)
                sp.dma_start(sc[:, i, 0:IK - 1], s[0:full].rearrange("(k p) -> p k", p=P)).then_inc(w_in, 16)
                sp.dma_start(sc[0:LASTI, i, IK - 1:IK], s[full:INTER].rearrange("(p k) -> p k", k=1)).then_inc(w_in, 16)
            sp.dma_start(down_raw[:, :, :], ins["L0_ffn_down_w"].rearrange("(k p) i -> p k i", p=P)).then_inc(w_in, 16)
            sp.dma_start(down_s[:, :], ins["L0_ffn_down_s"].rearrange("(k p) -> p k", p=P)).then_inc(w_in, 16)
            sp.dma_start(xin[:, :, :], xr[:, 0:CH, :]).then_inc(x_in, 16)
            with sp.Fori(1, PAIRS) as g:
                sp.wait_ge(res_done, 4 * g - 2)
                sp.dma_start(xin[:, :, :], xr[:, bass.ts(g, CH), :]).then_inc(x_in, 16)
                sp.wait_ge(ln_done, 2 * g)
                sp.dma_start(outr[:, bass.ts(g - 1, CH), :], fin[:, :, :]).then_inc(out_done, 16)
            sp.wait_ge(ln_done, 2 * PAIRS)
            sp.dma_start(outr[:, TILES - CH:TILES, :], fin[:, :, :]).then_inc(out_done, 16)
            sp.wait_ge(out_done, 16 * PAIRS)

        @block.tensor
        def _(pe):
            pe.wait_ge(w_in, 16 * 13)
            pe.wait_ge(scales_ready, 1)
            n = 0
            for i in range(2):
                for c in range(IK):
                    need(pe, w_copied, n - 7)
                    for k in range(KD):
                        mm = pe.transpose(bank[n % 8][:, k * P:k * P + rows(c)], raw[0:rows(c), i, c, k * P:(k + 1) * P],
                                          ident[0:rows(c), 0:rows(c)])
                    mm.then_inc(w_turned, 1)
                    n += 1
            for c in range(IK):
                need(pe, w_copied, n - 7)
                for k in range(KD):
                    mm = pe.transpose(bank[n % 8][0:rows(c), k * P:(k + 1) * P], down_raw[:, k, c * P:c * P + rows(c)],
                                      ident[:, :])
                mm.then_inc(w_turned, 1)
                n += 1
            pe.wait_ge(w_copied, 3 * IK)

            def group(g):
                for phase, count in ((0, FK), (1, IK)):
                    if phase == 0:
                        pe.wait_ge(h2_done, g + 1)
                    else:
                        pe.wait_ge(ln_done, 2 * g + 1)
                    src = h2 if phase == 0 else x2
                    for k in range(KD):
                        need(pe, hT_done, 4 * g + 2 * phase + k - 1)
                        for n in range(CH):
                            mm = pe.transpose(bank[k][:, n * P:(n + 1) * P], src[:, n, k * P:(k + 1) * P], ident[:, :])
                        mm.then_inc(turned, 1)
                    pe.wait_ge(hT_done, 4 * g + 2 * phase + 2)
                    for f in range(count):
                        m = P if phase == 0 else rows(f)
                        need(pe, gated, UNITS * g + FK * phase + f - 1)
                        for i in range(2):
                            w = (w1, w3)[i] if phase == 0 else gate_T[:, i, :, :]
                            for k in range(KD):
                                mm = pe.matmul(bank[2 + 2 * i + f % 2][0:m, :], w[:, k, f * P:f * P + m], hT[:, k, :],
                                               start=(k == 0), stop=(k == KD - 1))
                        mm.then_inc(up_mm, 1)
                    pe.wait_ge(gated, UNITS * g + FK + IK * phase)
                    for n in range(CH):
                        if n % 2 == 0:
                            need(pe, res_done, 4 * g + 2 * phase + n // 2 - 1)
                        for f in range(count):
                            m = P if phase == 0 else rows(f)
                            w = w2 if phase == 0 else down_T
                            mm = pe.matmul(bank[6 + n // 2][:, (n % 2) * D:(n % 2 + 1) * D], gT[0:m, f, n * P:(n + 1) * P],
                                           w[0:m, f, :], start=(f == 0), stop=(f == count - 1))
                        if n % 2:
                            mm.then_inc(down_mm, 1)

            group(0)
            with pe.Fori(1, PAIRS) as g:
                group(g)

        @block.scalar
        def _(act):
            for n in range(3 * IK):
                act.wait_ge(w_turned, n + 1)
                i, c = n // IK, n % IK
                if i < 2:
                    act.activation(gate_T[:, i, :, c * P:c * P + rows(c)],
                                   bank[n % 8][:, 0:KD * P].rearrange("p (k c) -> p k c", k=KD)[:, :, 0:rows(c)], ACT.Copy
                                   ).then_inc(w_copied, 1)
                else:
                    act.activation(down_T[0:rows(c), c, :], bank[n % 8][0:rows(c), 0:D], ACT.Copy).then_inc(w_copied, 1)

            def group(g):
                need(act, ms_done, g)
                for n in range(CH):
                    op = act.activation(sq[:, :], y_sb[:, bass.ds(CH * g + n, 1), :].rearrange("p o d -> p (o d)"),
                                        ACT.Square, accum_out=ssq[:, n:n + 1])
                    if n == CH - 1:
                        op.then_inc(ssq_done, 1)
                    act.drain()
                for phase, count in ((0, FK), (1, IK)):
                    for k in range(KD):
                        act.wait_ge(turned, 4 * g + 2 * phase + k + 1)
                        need(act, up_mm, UNITS * g + FK * phase)
                        if phase == 0:
                            op = act.activation(hT[:, k, :], bank[k][:, :], ACT.Copy, scale=n2w[:, k:k + 1])
                        else:
                            op = act.activation(hT[:, k, :], bank[k][:, :], ACT.Copy)
                        op.then_inc(hT_done, 1)
                    for f in range(count):
                        m = P if phase == 0 else rows(f)
                        u = UNITS * g + FK * phase + f
                        act.wait_ge(up_mm, u + 1)
                        need(act, gated, u - 1)
                        scale = 0.5 if phase == 0 else half_s[0:m, 0, f:f + 1]
                        act.activation(th[0:m, f % 2, :], bank[2 + f % 2][0:m, :], ACT.Tanh, scale=scale
                                       ).then_inc(tanh_done, 1)

            group(0)
            with act.Fori(1, PAIRS) as g:
                group(g)

        @block.gpsimd
        def _(pool):
            def group(g):
                pool.wait_ge(ms_done, g + 1)
                need(pool, h2_done, g)
                pool.tensor_tensor(rs[:, :], ms[:, :], powers[:, 1, 0:CH], ALU.pow).then_inc(rs_done, 1)
                for phase in range(2):
                    pool.wait_ge(var_done, 2 * g + phase + 1)
                    need(pool, ln_done, 2 * g + phase)
                    pool.tensor_tensor(rstd[:, :], var[:, :], powers[:, 1, 0:CH], ALU.pow).then_inc(rstd_done, 1)

            group(0)
            with pool.Fori(1, PAIRS) as g:
                group(g)

        @block.vector
        def _(dve):
            dve.wait_ge(w_in, 16 * 13)
            dve.tensor_scalar(half_s[:, 0, 0:IK - 1], sc[:, 0, 0:IK - 1], 0.5, None, ALU.mult)
            dve.tensor_scalar(half_s[0:LASTI, 0, IK - 1:IK], sc[0:LASTI, 0, IK - 1:IK], 0.5, None, ALU.mult)
            dve.drain()
            dve.tensor_tensor(half_s[:, 1, 0:IK - 1], half_s[:, 0, 0:IK - 1], sc[:, 1, 0:IK - 1], ALU.mult)
            dve.tensor_tensor(half_s[0:LASTI, 1, IK - 1:IK], half_s[0:LASTI, 0, IK - 1:IK], sc[0:LASTI, 1, IK - 1:IK],
                              ALU.mult)
            for k in range(KD):
                op = dve.tensor_scalar(down_raw[:, k, :], down_raw[:, k, :], down_s[:, k:k + 1], None, ALU.mult)
            op.then_inc(scales_ready, 1)

            def layernorm(dst, count, out_wait):
                for n in range(CH):
                    dve.bn_stats(stats[:, n, :], res[:, n, :])
                dve.drain()
                for n in range(CH):
                    dve.bn_aggr(mv[:, n, :], stats[:, n, :])
                dve.drain()
                dve.tensor_scalar(var[:, :].unsqueeze(2), mv[:, :, 1:2], LN_EPS, None, ALU.add).then_inc(var_done, 1)
                dve.wait_ge(rstd_done, count)
                need(dve, out_done, out_wait)
                for n in range(CH):
                    op = dve.tensor_scalar(dst[:, n, :], res[:, n, :], mv[:, n, 0:1], rstd[:, n:n + 1], ALU.subtract,
                                           ALU.mult)
                op.then_inc(ln_done, 1)
                dve.drain()

            def group(g):
                dve.wait_ge(ssq_done, g + 1)
                dve.tensor_scalar(ms[:, :], ssq[:, :], 1.0 / D, EPS, ALU.mult, ALU.add).then_inc(ms_done, 1)
                dve.wait_ge(rs_done, g + 1)
                need(dve, turned, 4 * g)
                for n in range(CH):
                    op = dve.tensor_scalar(h2[:, n, :], y_sb[:, bass.ds(CH * g + n, 1), :].rearrange("p o d -> p (o d)"),
                                           rs[:, n:n + 1], None, ALU.mult)
                op.then_inc(h2_done, 1)
                for phase, count in ((0, FK), (1, IK)):
                    for f in range(count):
                        m = P if phase == 0 else rows(f)
                        u = UNITS * g + FK * phase + f
                        dve.wait_ge(tanh_done, u + 1)
                        if f == 0:
                            need(dve, down_mm, 4 * g + 2 * phase)
                        dve.scalar_tensor_tensor(out=t1[0:m, f % 2, :], in0=th[0:m, f % 2, :], scalar=1.0,
                                                 in1=bank[2 + f % 2][0:m, :], op0=ALU.add, op1=ALU.mult)
                        dve.drain()
                        scale = 0.5 if phase == 0 else half_s[0:m, 1, f:f + 1]
                        dve.scalar_tensor_tensor(out=gT[0:m, f, :], in0=t1[0:m, f % 2, :], scalar=scale,
                                                 in1=bank[4 + f % 2][0:m, :], op0=ALU.mult, op1=ALU.mult
                                                 ).then_inc(gated, 1)
                    for i in range(2):
                        dve.wait_ge(down_mm, 4 * g + 2 * phase + i + 1)
                        if phase == 0:
                            base = y_sb[:, bass.ds(CH * g + 2 * i, 2), :]
                        else:
                            base = x2[:, 2 * i:2 * i + 2, :]
                        dst = res[:, 2 * i:2 * i + 2, :]
                        op = dve.tensor_tensor(dst, bank[6 + i][:, :].rearrange("p (n d) -> p n d", n=2), base, ALU.add)
                        if phase == 0:
                            dve.drain()
                            if i == 0:
                                dve.wait_ge(x_in, 16 * (g + 1))
                            op = dve.tensor_tensor(dst, dst, xin[:, 2 * i:2 * i + 2, :], ALU.add)
                        op.then_inc(res_done, 1)
                    dve.drain()
                    layernorm((x2, fin)[phase], 2 * g + phase + 1, 16 * g if phase else 0)

            group(0)
            with dve.Fori(1, PAIRS) as g:
                group(g)


INPUTS = ["L0_attn_x", "L0_attn_norm1_w", "L0_attn_wq", "L0_attn_wk", "L0_attn_wv", "L0_attn_conv_q", "L0_attn_conv_k",
          "L0_attn_conv_v", "L0_attn_f_a", "L0_attn_f_b", "L0_attn_A_log", "L0_attn_dt_bias", "L0_attn_b_w",
          "L0_attn_g_a", "L0_attn_g_b", "L0_attn_onorm_w", "L0_attn_wo", "L0_attn_norm2_w", "L0_attn_w1", "L0_attn_w2",
          "L0_attn_w3", "L0_ffn_gate_w", "L0_ffn_up_w", "L0_ffn_down_w", "L0_ffn_gate_s", "L0_ffn_up_s",
          "L0_ffn_down_s"]


def kernel(**inputs):
    import numpy as np
    import concourse.bacc as bacc
    from concourse.bass_utils import run_bass_kernel_spmd as run

    nc = bacc.Bacc("TRN2", target_bir_lowering=False, num_devices=1)
    arrays, aps = {}, {}

    def give(name, a):
        a = np.ascontiguousarray(a)
        arrays[f"in_{name}"] = a
        aps[name] = nc.dram_tensor(f"in_{name}", a.shape, mybir.dt.from_np(a.dtype), kind="ExternalInput").ap()

    for name in INPUTS:
        give(name, inputs[name])
    give("identity", np.eye(P, dtype=np.float32))
    give("level_masks", np.array([[[int(j // (2 * m) == i // m and j % (2 * m) < m) for i in range(HALF)]
                                   for m in (1 << l for l in range(LEVELS))] for j in range(P)], dtype=np.int32))
    out = nc.dram_tensor("out_0", (B, S, D), F32, kind="ExternalOutput").ap()
    delta_kernel(nc, aps, out)
    r = run(nc, [arrays], core_ids=[0])
    return r.results[0]["out_0"]
```
